# Optimizing a Trainium2 kernel written in Bass

```python
import numpy as np
import jax
import jax.numpy as jnp

def _softmax(x, axis=-1):
    return jax.nn.softmax(x, axis=axis)

def _gelu(x):
    return jax.nn.gelu(x, approximate=True)

def _silu(x):
    return jax.nn.silu(x)

def _sigmoid(x):
    return jax.nn.sigmoid(x)

def _layernorm(x, axis=-1, eps=1e-05):
    m = jnp.mean(x, axis=axis, keepdims=True)
    v = jnp.var(x, axis=axis, keepdims=True)
    return (x - m) / jnp.sqrt(v + eps)

def _scatter_add(tgt, idx, src, axis=0):
    return tgt.at[idx].add(src)

def _segment_sum(src, seg, n):
    return jax.ops.segment_sum(src, seg, n)
kernel_name = 'mk_gnn_resnorm_d1_gnn_r64_257264'

def setup_inputs(seed: int=0):
    np.random.seed(seed)
    _w = jnp.asarray

    def _rec_inputs():
        import jax
        import jax.numpy as jnp
        _gk = jax.random.key(seed)
        x = -0.001812 + 1 * jax.random.normal(jax.random.fold_in(_gk, 1), (100000, 32), jnp.float32)
        src = jax.random.randint(jax.random.fold_in(_gk, 2), (25000,), 0, 100000, jnp.int32)
        dst = jnp.minimum((100000 * jax.random.uniform(jax.random.fold_in(_gk, 3), (25000,)) ** 2.0).astype(jnp.int32), 99999)
        _o = jnp.argsort(dst, stable=True)
        src = src[_o]
        dst = dst[_o]
        edge_attr_10 = jax.random.uniform(jax.random.fold_in(_gk, 12), (25000, 10), jnp.float32, 0.0, 0.999998)
        edge_attr_3 = 0.00158508 + 0.999651 * jax.random.normal(jax.random.fold_in(_gk, 13), (25000, 3), jnp.float32)
        edge_weight = jax.random.uniform(jax.random.fold_in(_gk, 14), (25000,), jnp.float32, 0.0, 0.999997)
        return (x, src, dst, edge_attr_10, edge_attr_3, edge_weight)
    x, src, dst, edge_attr_10, edge_attr_3, edge_weight = _rec_inputs()

    def _L0_gnn_setup():
        import jax, jax.numpy as jnp
        import numpy as np
        SQRT3 = 3.0 ** 0.5

        def _mlp(emb, w1, w2):
            h = jax.nn.relu(emb @ w1 / jnp.sqrt(jnp.float32(w1.shape[0])))
            return h @ w2 / jnp.sqrt(jnp.float32(w2.shape[0]))
        key = jax.random.key(seed)
        ks = jax.random.split(key, 10)
        N, E = (10000, 2500)
        x = jax.random.normal(ks[0], (N, 32), jnp.float32)
        edge_src = jax.random.randint(ks[1], (E,), 0, N)
        edge_dst = jax.random.randint(ks[2], (E,), 0, N)
        edge_vec = jax.random.normal(ks[3], (E, 3), jnp.float32)
        emb = jax.random.uniform(ks[4], (E, 10), jnp.float32)
        norm = jax.random.uniform(ks[5], (E,), jnp.float32)
        fc1_w1 = jax.random.normal(ks[6], (10, 16), jnp.float32)
        fc1_w2 = jax.random.normal(ks[7], (16, 512), jnp.float32)
        fc2_w1 = jax.random.normal(ks[8], (10, 16), jnp.float32)
        fc2_w2 = jax.random.normal(ks[9], (16, 384), jnp.float32)
        return dict(x=x, edge_src=edge_src, edge_dst=edge_dst, edge_vec=edge_vec, emb=emb, norm=norm, num_nodes=N, fc1_w1=fc1_w1, fc1_w2=fc1_w2, fc2_w1=fc2_w1, fc2_w2=fc2_w2)
    _L0_gnn_all = _L0_gnn_setup()
    _L0_gnn_in = {k: v for k, v in _L0_gnn_all.items() if k in ('fc1_w1', 'fc1_w2', 'fc2_w1', 'fc2_w2')}
    del _L0_gnn_all
    return {'x': x, 'src': src, 'dst': dst, 'edge_attr_10': edge_attr_10, 'edge_attr_3': edge_attr_3, 'edge_weight': edge_weight, 'L0_gnn_fc1_w1': _L0_gnn_in['fc1_w1'], 'L0_gnn_fc1_w2': _L0_gnn_in['fc1_w2'], 'L0_gnn_fc2_w1': _L0_gnn_in['fc2_w1'], 'L0_gnn_fc2_w2': _L0_gnn_in['fc2_w2']}

def reference(x, src, dst, edge_attr_10, edge_attr_3, edge_weight, L0_gnn_fc1_w1, L0_gnn_fc1_w2, L0_gnn_fc2_w1, L0_gnn_fc2_w2):
    import jax
    import jax.numpy as jnp

    def _L0_gnn_ref(x, edge_src, edge_dst, edge_vec, emb, norm, num_nodes, fc1_w1, fc1_w2, fc2_w1, fc2_w2):
        import jax, jax.numpy as jnp
        import numpy as np
        SQRT3 = 3.0 ** 0.5

        def _mlp(emb, w1, w2):
            h = jax.nn.relu(emb @ w1 / jnp.sqrt(jnp.float32(w1.shape[0])))
            return h @ w2 / jnp.sqrt(jnp.float32(w2.shape[0]))
        E = edge_vec.shape[0]
        r = edge_vec / jnp.linalg.norm(edge_vec, axis=1, keepdims=True)
        sh1 = SQRT3 * r
        xs, xd = (x[edge_src], x[edge_dst])
        s1 = jnp.concatenate([xs[:, :8], xd[:, :8]], axis=1)
        v1 = jnp.concatenate([xs[:, 8:].reshape(E, 8, 3), xd[:, 8:].reshape(E, 8, 3)], axis=1)
        w = _mlp(emb, fc1_w1, fc1_w2)
        Wss = w[:, 0:128].reshape(E, 16, 8)
        Wvv = w[:, 128:256].reshape(E, 16, 8)
        Wsv = w[:, 256:384].reshape(E, 16, 8)
        Wvs = w[:, 384:512].reshape(E, 16, 8)
        a1 = 1.0 / jnp.sqrt(32.0)
        vdot1 = jnp.einsum('euk,ek->eu', v1, sh1) / SQRT3
        s_t = a1 * (jnp.einsum('eu,euw->ew', s1, Wss) + jnp.einsum('eu,euw->ew', vdot1, Wvv))
        v_t = a1 * (jnp.einsum('eu,euw->ew', s1, Wsv)[:, :, None] * sh1[:, None, :] + jnp.einsum('euk,euw->ewk', v1, Wvs))
        w2 = _mlp(emb, fc2_w1, fc2_w2)
        Ass = w2[:, 0:64].reshape(E, 8, 8)
        Avv = w2[:, 64:128].reshape(E, 8, 8)
        Bss = w2[:, 128:192].reshape(E, 8, 8)
        Bvv = w2[:, 192:256].reshape(E, 8, 8)
        Csv = w2[:, 256:320].reshape(E, 8, 8)
        Cvs = w2[:, 320:384].reshape(E, 8, 8)
        a2 = 1.0 / jnp.sqrt(16.0)
        vdot2 = jnp.einsum('euk,ek->eu', v_t, sh1) / SQRT3
        scal = a2 * (jnp.einsum('eu,euw->ew', s_t, Ass) + jnp.einsum('eu,euw->ew', vdot2, Avv))
        gates = a2 * (jnp.einsum('eu,euw->ew', s_t, Bss) + jnp.einsum('eu,euw->ew', vdot2, Bvv))
        vecs = a2 * (jnp.einsum('eu,euw->ew', s_t, Csv)[:, :, None] * sh1[:, None, :] + jnp.einsum('euk,euw->ewk', v_t, Cvs))
        edge_out = jnp.concatenate([jnp.tanh(scal), (vecs * jnp.tanh(gates)[:, :, None]).reshape(E, 24)], axis=1)
        edge_out = edge_out * norm[:, None]
        return jax.ops.segment_sum(edge_out, edge_dst, num_segments=num_nodes)
    x = _layernorm(x + _L0_gnn_ref(x, src, dst, edge_attr_3, edge_attr_10, edge_weight, 100000, L0_gnn_fc1_w1, L0_gnn_fc1_w2, L0_gnn_fc2_w1, L0_gnn_fc2_w2), axis=-1)
    return x

_drawn_inputs = setup_inputs


def setup_inputs(seed=0):
    import zlib

    import numpy as np

    out = dict(_drawn_inputs(seed))
    spreads = {}
    factors = {'edge_attr_10': 2.74, 'edge_attr_3': 3.092, 'edge_weight': 3.77}
    for name, (base, spread) in spreads.items():
        noise = np.random.default_rng([zlib.crc32(name.encode()), seed]).standard_normal(out[name].shape)
        drawn = base * np.exp(spread * noise) if base else spread * noise
        out[name] = jnp.asarray(drawn.astype(out[name].dtype))
    for name, factor in factors.items():
        out[name] = (out[name] * factor).astype(out[name].dtype)
    return out
```

```python
from contextlib import ExitStack

import concourse.bass as bass
from concourse import mybir

F32 = mybir.dt.float32
I32 = mybir.dt.int32
BF16 = mybir.dt.bfloat16
ALU = mybir.AluOpType
ACT = mybir.ActivationFunctionType
AX_X = mybir.AxisListType.X

P = 128
DF = 32
TPC = 4
HID = 16
NE10, NE3 = 10, 3
NB = 9
NSC = 16
FAR = 200000.0
WIN = 512
WPS = 4
SUP = WIN * WPS
SQRT3 = 3.0 ** 0.5
EPS = 1e-5


def gnn_layernorm(nc, x, src, dst, emb, vec, weight, fc1_w1, fc1_w2, fc2_w1, fc2_w2, out):
    N = x.shape[0]
    E = src.shape[0]
    NT = -(-E // P)
    NTP = NT + TPC
    NCH = NT // TPC
    NW = -(-N // WIN)
    NS = -(-N // SUP)
    assert NT % TPC == 0 and NT > P and NTP <= 2 * P and NCH % 2 == 1 and NS % 2 == 1
    full1 = E // P - P
    rest = E % P

    with ExitStack() as ctx:
        def sb(name, shape, dt=F32):
            return ctx.enter_context(nc.sbuf_tensor(name, shape, dt))

        def sem(name):
            return ctx.enter_context(nc.semaphore(name))

        bank = [ctx.enter_context(nc.psum_tensor(f"bank{i}", [P, 512], F32)) for i in range(8)]

        ident = sb("ident", [P, P])
        sel_base = sb("sel_base", [P, 8])
        sel_layer1 = sb("sel_layer1", [P, 4, 8])
        sel_layer2 = sb("sel_layer2", [P, 8])
        node_of_col = sb("node_of_col", [P, WIN])
        window_base = sb("window_base", [P, NW])
        zeros = sb("zeros", [P, 512], BF16)
        dst_raw = sb("dst_raw", [P, 2, P], I32)
        src_raw = sb("src_raw", [P, 2, P], I32)
        dst_tile = sb("dst_tile", [P, 2, P])
        src_tile = sb("src_tile", [P, 2, P])
        nrm_tile = sb("nrm_tile", [P, 2, P])
        vec_tile = sb("vec_tile", [P, 2, P, NE3])
        emb_tile = sb("emb_tile", [P, 2, P, NE10])
        edge_in = sb("edge_in", [P, NTP, NE10 + NSC])
        vec_row = sb("vec_row", [P, NTP, NE3])
        vec_sq = sb("vec_sq", [P, NTP, NE3])
        vec_ss = sb("vec_ss", [P, NTP])
        vec_len = sb("vec_len", [P, NTP])
        vec_inv = sb("vec_inv", [P, NTP])
        dirn = sb("dirn", [P, NTP, NE3])
        nrm_row = sb("nrm_row", [P, NTP])
        dst_row = sb("dst_row", [P, NTP])
        idx = sb("idx", [P, NTP, 2], I32)
        w1_raw = sb("w1_raw", [TPC * NE10, 2, TPC, HID])
        w1_rep = sb("w1_rep", [TPC * NE10, 2, TPC, P])
        w_layer1 = sb("w_layer1", [P, 4, P])
        w_layer2 = sb("w_layer2", [P, 5, P])
        span = sb("span", [P, 2, 2])
        tile_no = sb("tile_no", [P, 256])
        tile_rev = sb("tile_rev", [P, 256])
        win_lo = sb("win_lo", [P, 2])
        win_hi = sb("win_hi", [P, 2])
        touch_a = sb("touch_a", [P, 2, 256])
        touch_b = sb("touch_b", [P, 2, 256])
        touch = sb("touch", [P, 2, 256])
        mark = sb("mark", [P, 2, 2, 256])
        bound = sb("bound", [P, 2, 2])
        row = sb("row", [1, 8, 256])
        table = sb("table", [1, 2, 256], I32)
        idx_now = sb("idx_now", [P, 2, TPC, 2], I32)
        feat = sb("feat", [P, 2, TPC, P])
        vdot_k = sb("vdot_k", [P, TPC, 2, 8, 3])
        emb_now = sb("emb_now", [P, 2, TPC, NE10])
        scale_now = sb("scale_now", [P, 2, TPC, NSC, 8])
        feat_t = sb("feat_t", [P, 2, 512])
        emb_t = sb("emb_t", [TPC * NE10, 2, P])
        scale_t = sb("scale_t", [P, 2, 512])
        hid = sb("hid", [P, 2, 2, 512])
        prod = sb("prod", [P, 3, 512])
        feat2 = sb("feat2", [P, 2, 512])
        tanh_out = sb("tanh_out", [P, 2, TPC, 16])
        gate = sb("gate", [P, 2, TPC, 8])
        vals = sb("vals", [P, NTP, DF])
        onehot = sb("onehot", [P, 2, WIN])
        xin = sb("xin", [P, 2, 16, DF])
        ysum = sb("ysum", [P, 2, 16, DF])
        mean = sb("mean", [P, 2, 16])
        nmean = sb("nmean", [P, 2, 16])
        cent = sb("cent", [P, 2, 16, DF])
        csq = sb("csq", [P, 2, 16, DF])
        var = sb("var", [P, 2, 16])
        stdev = sb("stdev", [P, 2, 16])
        rstd = sb("rstd", [P, 2, 16])
        eps = sb("eps", [P, 1])
        yout = sb("yout", [P, 2, 16, DF])

        s_clear = sem("s_clear")
        s_attr = sem("s_attr")
        s_wts = sem("s_wts")
        s_ident0 = sem("s_ident0")
        s_const = sem("s_const")
        s_pre = sem("s_pre")
        s_zero = sem("s_zero")
        s_turn = sem("s_turn")
        s_moved = sem("s_moved")
        s_spanT = sem("s_spanT")
        s_boundT = sem("s_boundT")
        s_staged = sem("s_staged")
        s_gath = [sem(f"s_gath{i}") for i in range(2)]
        s_prep = sem("s_prep")
        s_now = sem("s_now")
        s_featT = sem("s_featT")
        s_scaleT = sem("s_scaleT")
        s_embT = sem("s_embT")
        s_featS = sem("s_featS")
        s_scaleS = sem("s_scaleS")
        s_embS = sem("s_embS")
        s_hidP = sem("s_hidP")
        s_hidS = sem("s_hidS")
        s_u = sem("s_u")
        s_p = sem("s_p")
        s_red = sem("s_red")
        s_f2 = sem("s_f2")
        s_tanh = sem("s_tanh")
        s_out = sem("s_out")
        s_x = [sem(f"s_x{i}") for i in range(2)]
        s_oh = [sem(f"s_oh{i}") for i in range(2)]
        s_ohused = [sem(f"s_ohused{i}") for i in range(2)]
        s_agg0 = sem("s_agg0")
        s_y = sem("s_y")
        s_sum = sem("s_sum")
        s_mean = sem("s_mean")
        s_cent = sem("s_cent")
        s_csq = sem("s_csq")
        s_var = sem("s_var")
        s_sd = sem("s_sd")
        s_len = sem("s_len")
        s_rstd = sem("s_rstd")
        s_yout = sem("s_yout")
        s_store = [sem(f"s_store{i}") for i in range(2)]

        block = ctx.enter_context(nc.Block())
        n_attr, n_wts = 0, 0

        def weight_pieces():
            def cols(w, off, u0):
                return w[:, off + 8 * u0:off + 8 * u0 + 64].rearrange("h (u o) -> u h o", o=8)

            for side in range(2):
                r = 32 * side
                yield w_layer1[r:r + 8, 0, :], cols(fc1_w2, 0, 8 * side)
                yield w_layer1[64 + 8 * side:72 + 8 * side, 0, :], cols(fc1_w2, 128, 8 * side)
                for k in range(3):
                    yield w_layer1[r + 8 + k:r + 8 + k + 22:3, 1 + k, :], cols(fc1_w2, 384, 8 * side)
                    s = 80 + 16 * k + 8 * side
                    yield w_layer1[s:s + 8, 1 + k, :], cols(fc1_w2, 256, 8 * side)
            for b, (ss, vv) in enumerate(((0, 64), (128, 192))):
                yield w_layer2[0:8, b, :], cols(fc2_w2, ss, 0)
                for k in range(3):
                    r = 32 * (k + 1) + 8
                    yield w_layer2[r:r + 8, b, :], cols(fc2_w2, vv, 0)
            for k in range(3):
                yield w_layer2[8 + 8 * k:16 + 8 * k, 2 + k, :], cols(fc2_w2, 256, 0)
                r = 32 * (k + 1)
                yield w_layer2[r:r + 8, 2 + k, :], cols(fc2_w2, 320, 0)

        pieces = list(weight_pieces())
        n_wts = 16 * (len(pieces) + 2 * TPC)
        n_attr = 16 * 15

        def attribute(eng, raw, flat, w):
            a = flat if w == 1 else flat.rearrange("e k -> (e k)")
            raw = raw.rearrange("p b e -> p b e") if w == 1 else raw.rearrange("p b e k -> p b (e k)")
            L = P * w
            eng.dma_start(raw[:, 0, :], a[0:P * L].rearrange("(t e) -> t e", e=L)).then_inc(s_attr, 16)
            eng.dma_start(raw[0:full1, 1, :],
                          a[P * L:(P + full1) * L].rearrange("(t e) -> t e", e=L)).then_inc(s_attr, 16)
            eng.dma_start(raw[full1:full1 + 1, 1, 0:rest * w],
                          a[(P + full1) * L:E * w].rearrange("(t e) -> t e", t=1)).then_inc(s_attr, 16)

        def rows_of(dram, s0, parts=P, nw=WPS, w0=0):
            base = s0 * SUP + w0 * WIN
            return dram[bass.ds(base, nw * parts * 4), :].rearrange("(w p b) f -> p w (b f)", w=nw, b=4)

        def last_parts():
            left = N - (NS - 1) * SUP
            full = left // WIN
            part = (left - full * WIN) // 4
            assert part * 4 + full * WIN == left
            return full, part

        @block.sync
        def _(sp):
            sp.wait_ge(s_clear, 7)
            attribute(sp, dst_raw, dst, 1)
            attribute(sp, src_raw, src, 1)
            attribute(sp, vec_tile, vec, NE3)
            attribute(sp, nrm_tile, weight, 1)
            attribute(sp, emb_tile, emb, NE10)
            for layer, w in enumerate((fc1_w1, fc2_w1)):
                for g in range(TPC):
                    sp.dma_start(w1_raw[NE10 * g:NE10 * g + NE10, layer, g, :], w[:, :]).then_inc(s_wts, 16)
            for piece, cols in pieces:
                sp.dma_start(piece.rearrange("p (h o) -> p h o", o=8), cols).then_inc(s_wts, 16)

            def load(s, slot, first):
                if not first:
                    sp.wait_ge(s_y, s - 1)
                sp.dma_start(xin[:, slot, :, :].rearrange("p (w b) f -> p w (b f)", w=WPS),
                             rows_of(x, s)).then_inc(s_x[slot], 16)

            def load_last(s, slot):
                full, part = last_parts()
                sp.wait_ge(s_y, s - 1)
                sp.dma_start(xin[:, slot, 0:4 * full, :].rearrange("p (w b) f -> p w (b f)", w=full),
                             rows_of(x, s, P, full)).then_inc(s_x[slot], 16)
                sp.dma_start(xin[0:part, slot, 4 * full:4 * full + 4, :].rearrange("p (w b) f -> p w (b f)", w=1),
                             rows_of(x, s, part, 1, full)).then_inc(s_x[slot], 16)

            def store(s, slot):
                sp.wait_ge(s_yout, s + 1)
                sp.dma_start(rows_of(out, s), yout[:, slot, :, :].rearrange("p (w b) f -> p w (b f)", w=WPS))\
                    .then_inc(s_store[slot], 16)

            load(0, 0, True)
            load(1, 1, True)
            with sp.Fori(0, (NS - 3) // 2) as i:
                for slot in range(2):
                    load(i * 2 + slot + 2, slot, False)
                    store(i * 2 + slot, slot)
            load_last(NS - 1, 0)
            store(NS - 3, 0)
            store(NS - 2, 1)
            sp.wait_ge(s_yout, NS)
            full, part = last_parts()
            sp.dma_start(rows_of(out, NS - 1, P, full),
                         yout[:, 0, 0:4 * full, :].rearrange("p (w b) f -> p w (b f)", w=full)).then_inc(s_store[0], 16)
            sp.dma_start(rows_of(out, NS - 1, part, 1, full),
                         yout[0:part, 0, 4 * full:4 * full + 4, :].rearrange("p (w b) f -> p w (b f)", w=1))\
                .then_inc(s_store[0], 16)
            sp.wait_ge(s_store[0], 16 * ((NS - 1) // 2 + 2))
            sp.wait_ge(s_store[1], 16 * ((NS - 1) // 2))

        @block.gpsimd
        def _(pool):
            pool.memset(ident[:, :], 0.0).then_inc(s_ident0, 1)
            pool.memset(w_layer1[:, :, :], 0.0).then_inc(s_clear, 1)
            pool.memset(w_layer2[:, :, :], 0.0).then_inc(s_clear, 1)
            pool.wait_ge(s_ident0, 1)
            pool.affine_select(out=ident[:, :], in_=ident[:, :], compare_op=ALU.not_equal, fill=1.0,
                               base=0, pattern=[[-1, P]], channel_multiplier=1).then_inc(s_const, 1)
            pool.iota(tile_no[:, :], [[1, 256]], base=1, channel_multiplier=0,
                      allow_small_or_imprecise_dtypes=True).then_inc(s_const, 1)
            pool.iota(tile_rev[:, :], [[-1, 256]], base=256, channel_multiplier=0,
                      allow_small_or_imprecise_dtypes=True).then_inc(s_const, 1)
            for b in range(2):
                pool.iota(win_lo[:, b:b + 1], [[1, 1]], base=b * P * WIN, channel_multiplier=WIN,
                          allow_small_or_imprecise_dtypes=True).then_inc(s_const, 1)
                pool.iota(win_hi[:, b:b + 1], [[1, 1]], base=b * P * WIN + WIN - 1, channel_multiplier=WIN,
                          allow_small_or_imprecise_dtypes=True).then_inc(s_const, 1)
            pool.iota(node_of_col[:, :].rearrange("p (b c) -> p b c", b=4), [[1, 4], [4, P]], base=0,
                      channel_multiplier=0, allow_small_or_imprecise_dtypes=True).then_inc(s_const, 1)
            pool.iota(window_base[:, :], [[WIN, NW]], base=0, channel_multiplier=0,
                      allow_small_or_imprecise_dtypes=True).then_inc(s_const, 1)

            def gather(c, slot, first):
                if not first:
                    pool.wait_ge(s_gath[slot], (c - slot) * 64)
                pool.tensor_copy(idx_now[:, slot, :, :], idx[:, bass.ds(c * TPC, TPC), :]).then_inc(s_staged, 1)
                if not first:
                    pool.wait_ge(s_featT, c - 1)
                pool.wait_ge(s_staged, c + 1)
                if not first:
                    pool.nop(nofuse=True)
                for g in range(TPC):
                    for side in range(2):
                        pool.indirect_dma_start(
                            feat[:, slot, g, DF * side:DF * side + DF], None, x[:, :],
                            bass.IndirectOffsetOnAxis(ap=idx_now[:, slot, g, side:side + 1], axis=0),
                        ).then_inc(s_gath[slot], 16)

            pool.wait_ge(s_pre, 3)
            gather(0, 0, True)
            gather(1, 1, True)
            with pool.Fori(1, NCH // 2) as i:
                for slot in range(2):
                    gather(i * 2 + slot, slot, False)
            gather(NCH - 1, 0, False)

            def centre(s, slot, first):
                pool.wait_ge(s_mean, s + 1)
                if not first:
                    pool.wait_ge(s_csq, s - 1)
                    pool.wait_ge(s_yout, s - 1)
                pool.tensor_tensor(cent[:, slot, :, :], ysum[:, slot, :, :],
                                   nmean[:, slot, :].unsqueeze(2).broadcast_to([P, 16, DF]), ALU.add)\
                    .then_inc(s_cent, 1)

            def scale(s, slot, first):
                pool.wait_ge(s_rstd, s + 1)
                if not first:
                    pool.wait_ge(s_store[slot], (s - slot) * 8)
                pool.tensor_tensor(yout[:, slot, :, :], cent[:, slot, :, :],
                                   rstd[:, slot, :].unsqueeze(2).broadcast_to([P, 16, DF]), ALU.mult)\
                    .then_inc(s_yout, 1)

            centre(0, 0, True)
            centre(1, 1, True)
            scale(0, 0, True)
            centre(2, 0, False)
            scale(1, 1, True)
            centre(3, 1, False)
            with pool.Fori(2, (NS - 1) // 2) as i:
                for slot in range(2):
                    scale(i * 2 + slot - 2, slot, False)
                    centre(i * 2 + slot, slot, False)
            scale(NS - 3, 0, False)
            centre(NS - 1, 0, False)
            scale(NS - 2, 1, False)
            scale(NS - 1, 0, False)

        @block.scalar
        def _(act):
            def now(c, slot, first):
                if not first:
                    act.wait_ge(s_embT, c - 1)
                act.activation(emb_now[:, slot, :, :], edge_in[:, bass.ds(c * TPC, TPC), 0:NE10], ACT.Copy)\
                    .then_inc(s_now, 1)
                if not first:
                    act.wait_ge(s_scaleT, c - 1)
                act.activation(scale_now[:, slot, :, :, :],
                               edge_in[:, bass.ds(c * TPC, TPC), NE10:].unsqueeze(3).broadcast_to([P, TPC, NSC, 8]),
                               ACT.Copy).then_inc(s_now, 1)

            def evacuate(c, slot, first):
                act.wait_ge(s_featT, c + 1)
                if not first:
                    act.wait_ge(s_u, c * NB - 14)
                act.activation(feat_t[:, slot, :], bank[0][:, :], ACT.Copy).then_inc(s_featS, 1)
                act.wait_ge(s_embT, c + 1)
                if not first:
                    act.wait_ge(s_hidP, c * 2 - 2)
                act.activation(emb_t[:, slot, :], bank[7][0:TPC * NE10, 0:P], ACT.Copy).then_inc(s_embS, 1)
                act.wait_ge(s_scaleT, c + 1)
                if not first:
                    act.wait_ge(s_f2, c - 1)
                act.activation(scale_t[:, slot, :], bank[1][:, :], ACT.Copy).then_inc(s_scaleS, 1)

            def relu(c, slot, layer, first):
                act.wait_ge(s_hidP, c * 2 + layer + 1)
                if not first:
                    act.wait_ge(s_p, c * NB - (14 if layer == 0 else 9))
                act.activation(hid[:, slot, layer, :], bank[2][:, :], ACT.Relu, scale=NE10 ** -0.5)\
                    .then_inc(s_hidS, 1)

            def tanh(c, slot, first):
                act.wait_ge(s_red, c * NB + NB)
                if not first:
                    act.wait_ge(s_out, c * 3 - 3)
                o2 = bank[6][:, 0:TPC * 40].rearrange("p (g c) -> p g c", g=TPC)
                act.activation(tanh_out[:, slot, :, :], o2[:, :, 0:16], ACT.Tanh).then_inc(s_tanh, 1)

            def ahead(c, slot, first):
                now(c, slot, first)
                evacuate(c, slot, first)
                relu(c, slot, 0, first)
                relu(c, slot, 1, first)

            act.wait_ge(s_pre, 6)
            act.activation(vec_len[:, :], vec_ss[:, :], ACT.Sqrt).then_inc(s_len, 1)
            act.wait_ge(s_pre, 8)
            ahead(0, 0, True)
            ahead(1, 1, True)
            tanh(0, 0, True)
            ahead(2, 0, False)
            tanh(1, 1, True)
            with act.Fori(1, NCH // 2) as i:
                ahead(i * 2 + 1, 1, False)
                tanh(i * 2, 0, False)
                ahead(i * 2 + 2, 0, False)
                tanh(i * 2 + 1, 1, False)
            tanh(NCH - 1, 0, False)

            def square(s, slot, first):
                act.wait_ge(s_cent, s + 1)
                if not first:
                    act.wait_ge(s_var, s - 1)
                act.activation(csq[:, slot, :, :], cent[:, slot, :, :], ACT.Square, scale=DF ** -0.5)\
                    .then_inc(s_csq, 1)

            def root(s, slot, first):
                act.wait_ge(s_var, s + 1)
                if not first:
                    act.wait_ge(s_rstd, s - 1)
                act.activation(stdev[:, slot, :], var[:, slot, :], ACT.Sqrt, bias=eps[:, :]).then_inc(s_sd, 1)

            square(0, 0, True)
            square(1, 1, True)
            root(0, 0, True)
            square(2, 0, False)
            root(1, 1, True)
            square(3, 1, False)
            root(2, 0, False)
            with act.Fori(2, (NS - 1) // 2) as i:
                for slot in range(2):
                    square(i * 2 + slot, slot, False)
                    root(i * 2 + slot - 1, 1 - slot, False)
            square(NS - 1, 0, False)
            root(NS - 2, 1, False)
            root(NS - 1, 0, False)

        @block.tensor
        def _(pe):
            pe.wait_ge(s_const, 1)
            pe.wait_ge(s_attr, n_attr)
            pe.wait_ge(s_clear, 9)
            attrs = [emb_tile[:, :, :, k] for k in range(NE10)] + [vec_tile[:, :, :, k] for k in range(NE3)]
            attrs += [nrm_tile, dst_tile, src_tile]
            for a, t in enumerate(attrs):
                for b in range(2):
                    col = (a % 2) * 256 + b * P
                    last = pe.transpose(bank[a // 2][:, col:col + P], t[:, b, :], ident[:, :])
            last.then_inc(s_turn, 1)
            pe.wait_ge(s_pre, 1)
            pe.wait_ge(s_moved, 1)
            for j in range(2):
                for b in range(2):
                    last = pe.matmul(bank[0][:, j * 256 + b * P:j * 256 + b * P + P],
                                     span[:, b, j:j + 1].broadcast_to([P, P]), ident[:, :], start=True, stop=True)
            last.then_inc(s_spanT, 1)
            pe.wait_ge(s_pre, 12)
            for j in range(2):
                for b in range(2):
                    last = pe.matmul(bank[1][0:1, j * 256 + b * P:j * 256 + b * P + P],
                                     bound[:, b, j:j + 1], ident[:, :], start=True, stop=True)
            last.then_inc(s_boundT, 1)
            pe.wait_ge(s_pre, 20)

            def turn(c, slot, first):
                pe.wait_ge(s_prep, c * 3 + 3)
                if not first:
                    pe.wait_ge(s_featS, c)
                    pe.wait_ge(s_embS, c)
                pe.wait_ge(s_now, c * 2 + 1)
                for g in range(TPC):
                    last = pe.transpose(bank[0][:, g * P:g * P + P], feat[:, slot, g, :], ident[:, :])
                last.then_inc(s_featT, 1)
                pe.transpose(bank[7][0:TPC * NE10, 0:P], emb_now[:, slot, :, :].rearrange("p g k -> p (g k)"), ident[:, :])\
                    .then_inc(s_embT, 1)
                if not first:
                    pe.wait_ge(s_scaleS, c)
                pe.wait_ge(s_now, c * 2 + 2)
                for g in range(TPC):
                    last = pe.transpose(bank[1][:, g * P:g * P + P],
                                        scale_now[:, slot, g, :, :].rearrange("p m o -> p (m o)"), ident[:, :])
                last.then_inc(s_scaleT, 1)

            def hidden(c, slot, layer, first):
                pe.wait_ge(s_embS, c + 1)
                if not (first and layer == 0):
                    pe.wait_ge(s_hidS, c * 2 + layer)
                for g in range(TPC):
                    last = pe.matmul(bank[2][:, g * P:g * P + P], w1_rep[:, layer, g, :], emb_t[:, slot, :],
                                     start=True, stop=True)
                last.then_inc(s_hidP, 1)

            def weigh(c, slot, b):
                n = c * NB + b
                ub = bank[4 + (slot + b) % 2]
                if not (isinstance(c, int) and c * NB + b < 2):
                    pe.wait_ge(s_p, n - 1)
                if b < 4:
                    if b == 0:
                        pe.wait_ge(s_featS, c + 1)
                    pe.matmul(ub[:, :], w_layer1[:, b, :], feat_t[:, slot, :], start=True, stop=True)\
                        .then_inc(s_u, 1)
                else:
                    if b == 4:
                        pe.wait_ge(s_f2, c + 1)
                    pe.matmul(ub[:, :], w_layer2[:, b - 4, :], feat2[:, slot, :], start=True, stop=True)\
                        .then_inc(s_u, 1)

            def reduce(c, slot, b):
                pe.wait_ge(s_p, c * NB + b + 1)
                pb = prod[:, b % 3, :]
                if b < 4:
                    if b == 0:
                        if not (isinstance(c, int) and c == 0):
                            pe.wait_ge(s_f2, c)
                    pe.matmul(bank[3][32 * b:32 * b + 32, :], sel_layer1[:, :, :].rearrange("p m o -> p (m o)"),
                              pb, start=True, stop=True).then_inc(s_red, 1)
                else:
                    if b == 4:
                        if not (isinstance(c, int) and c == 0):
                            pe.wait_ge(s_out, c * 3)
                    for g in range(TPC):
                        at = g * 40 + 8 * (b - 4)
                        last = pe.matmul(bank[6][:, at:at + 8], pb[:, g * P:g * P + P], sel_layer2[:, :],
                                         start=True, stop=True)
                    last.then_inc(s_red, 1)

            def chunk(c, slot, nxt, first_next):
                weigh(c, slot, 0)
                weigh(c, slot, 1)
                reduce(c, slot, 0)
                weigh(c, slot, 2)
                reduce(c, slot, 1)
                weigh(c, slot, 3)
                reduce(c, slot, 2)
                if nxt:
                    turn(c + 1, 1 - slot, first_next)
                reduce(c, slot, 3)
                weigh(c, slot, 4)
                weigh(c, slot, 5)
                reduce(c, slot, 4)
                if nxt:
                    hidden(c + 1, 1 - slot, 0, first_next)
                weigh(c, slot, 6)
                reduce(c, slot, 5)
                weigh(c, slot, 7)
                reduce(c, slot, 6)
                if nxt:
                    hidden(c + 1, 1 - slot, 1, first_next)
                weigh(c, slot, 8)
                reduce(c, slot, 7)
                reduce(c, slot, 8)

            turn(0, 0, True)
            hidden(0, 0, 0, True)
            hidden(0, 0, 1, True)
            chunk(0, 0, True, False)
            chunk(1, 1, True, False)
            with pe.Fori(1, NCH // 2) as i:
                chunk(i * 2, 0, True, False)
                chunk(i * 2 + 1, 1, True, False)
            chunk(NCH - 1, 0, False, False)

            pe.wait_ge(s_out, NCH * 3)
            pe.wait_ge(s_zero, 1)

            def sums(s, slot, nwin, first):
                agg = bank[slot]
                if not first:
                    pe.wait_ge(s_y, s - 1)
                pe.matmul(agg[:, :], zeros[:, 0:P], zeros[:, :], start=True, stop=True,
                          skip_group_check=True).then_inc(s_agg0, 1)
                for w in range(nwin):
                    n0 = pe.value_load(table[0:1, 0, bass.ds(s * WPS + w, 1)], min_val=0, max_val=NT * NW)
                    n1 = pe.value_load(table[0:1, 0, bass.ds(s * WPS + w + 1, 1)], min_val=1, max_val=NT * NW)
                    off = pe.value_load(table[0:1, 1, bass.ds(s * WPS + w, 1)], min_val=-2 * NT * NW, max_val=NT)
                    with pe.Fori(n0, n1) as n:
                        t = nc.s_assert_within(pe.snap(n * 2 + off), 0, NT,
                                              skip_runtime_bounds_check_because="the table's tiles lie in [0, NT)")
                        for h in range(2):
                            pe.wait_ge(s_oh[h], n + 1)
                            for b in range(4):
                                last = pe.matmul(agg[:, (w * 4 + b) * DF:(w * 4 + b + 1) * DF],
                                                 onehot[:, h, b * P:b * P + P], vals[:, bass.ds(t + h, 1), :],
                                                 start=False, stop=False, skip_group_check=True)
                            last.then_inc(s_ohused[h], 1)

            sums(0, 0, WPS, True)
            sums(1, 1, WPS, True)
            with pe.Fori(1, (NS - 1) // 2) as i:
                for slot in range(2):
                    sums(i * 2 + slot, slot, WPS, False)
            sums(NS - 1, 0, NW - (NS - 1) * WPS, False)

        @block.vector
        def _(dve):
            dve.memset(dst_raw[:, :, :], int(FAR)).then_inc(s_clear, 1)
            dve.memset(src_raw[:, :, :], 0).then_inc(s_clear, 1)
            dve.memset(nrm_tile[:, :, :], 0.0).then_inc(s_clear, 1)
            dve.memset(vec_tile[:, :, :, :], 1.0).then_inc(s_clear, 1)
            dve.memset(emb_tile[:, :, :, :], 0.0)
            dve.memset(eps[:, :], EPS)
            dve.memset(w1_raw[:, :, :, :], 0.0).then_inc(s_clear, 1)
            dve.memset(vals[:, NT:NTP, :], 0.0)
            dve.memset(edge_in[:, :, NE10:], 0.0)
            dve.memset(zeros[:, :], 0.0).then_inc(s_zero, 1)
            dve.wait_ge(s_zero, 1)
            dve.memset(edge_in[:, :, NE10::4], 1.0)
            for h in range(2):
                dve.memset(onehot[:, h, :], 0.0).then_inc(s_ohused[h], 1)
            dve.wait_ge(s_attr, n_attr)
            dve.tensor_copy(dst_tile[:, :, :], dst_raw[:, :, :]).then_inc(s_clear, 1)
            dve.tensor_copy(src_tile[:, :, :], src_raw[:, :, :]).then_inc(s_clear, 1)
            dve.wait_ge(s_clear, 9)
            dve.tensor_reduce(span[:, :, 0:1], dst_tile[:, :, :], AX_X, ALU.min)
            dve.tensor_reduce(span[:, :, 1:2], dst_tile[:, :, :], AX_X, ALU.max).then_inc(s_pre, 1)
            dve.wait_ge(s_turn, 1)

            def turned(a):
                return bank[a // 2][:, (a % 2) * 256:(a % 2) * 256 + NTP]

            dve.tensor_scalar(idx[:, :, 1], turned(14), float(N - 1), None, ALU.min).then_inc(s_pre, 1)
            dve.tensor_copy(idx[:, :, 0], turned(15)).then_inc(s_pre, 1)
            for k in range(NE10):
                ins = dve.tensor_copy(edge_in[:, :, k], turned(k))
                if k == 1:
                    ins.then_inc(s_moved, 1)
            for k in range(NE3):
                dve.tensor_copy(vec_row[:, :, k], turned(NE10 + k))
            dve.tensor_copy(nrm_row[:, :], turned(13))
            dve.tensor_copy(dst_row[:, :], turned(14)).then_inc(s_pre, 1)
            dve.wait_ge(s_pre, 4)
            dve.tensor_tensor(vec_sq[:, :, :], vec_row[:, :, :], vec_row[:, :, :], ALU.mult).then_inc(s_pre, 1)
            dve.wait_ge(s_pre, 5)
            dve.tensor_reduce(vec_ss[:, :], vec_sq[:, :, :], AX_X, ALU.add).then_inc(s_pre, 1)
            dve.wait_ge(s_len, 1)
            dve.reciprocal(vec_inv[:, :], vec_len[:, :]).then_inc(s_pre, 1)
            dve.wait_ge(s_pre, 7)
            inv = vec_inv[:, :].unsqueeze(2).broadcast_to([P, NTP, NE3])
            dve.tensor_tensor(dirn[:, :, :], vec_row[:, :, :], inv, ALU.mult)
            dve.tensor_tensor(edge_in[:, :, NE10 + 5::4], vec_row[:, :, :], inv, ALU.mult)
            dve.scalar_tensor_tensor(out=edge_in[:, :, NE10 + 1:NE10 + 4], in0=vec_row[:, :, :], scalar=SQRT3,
                                     in1=inv, op0=ALU.mult, op1=ALU.mult).then_inc(s_pre, 1)
            dve.wait_ge(s_spanT, 1)
            dve.wait_ge(s_const, 9)
            for b in range(2):
                dve.tensor_scalar(touch_a[:, b, :], bank[0][:, 0:256], win_hi[:, b:b + 1], None, ALU.is_le)
                ins = dve.tensor_scalar(touch_b[:, b, :], bank[0][:, 256:512], win_lo[:, b:b + 1], None, ALU.is_ge)
            ins.then_inc(s_pre, 1)
            dve.wait_ge(s_pre, 9)
            dve.tensor_tensor(touch[:, :, :], touch_a[:, :, :], touch_b[:, :, :], ALU.mult).then_inc(s_pre, 1)
            dve.wait_ge(s_pre, 10)
            for b in range(2):
                dve.tensor_tensor(mark[:, b, 0, :], touch[:, b, :], tile_rev[:, :], ALU.mult)
                ins = dve.tensor_tensor(mark[:, b, 1, :], touch[:, b, :], tile_no[:, :], ALU.mult)
            ins.then_inc(s_pre, 1)
            dve.wait_ge(s_pre, 11)
            dve.tensor_reduce(bound[:, :, :], mark[:, :, :, :], AX_X, ALU.max).then_inc(s_pre, 1)
            dve.wait_ge(s_boundT, 1)
            dve.tensor_scalar(row[:, 0, :], bank[1][0:1, 0:256], -1.0, 256.0, ALU.mult, ALU.add).then_inc(s_pre, 1)
            dve.wait_ge(s_pre, 13)
            dve.tensor_scalar(row[:, 1, :], row[:, 0, :], float(NT - 1), None, ALU.min).then_inc(s_pre, 1)
            dve.wait_ge(s_pre, 14)
            dve.tensor_tensor(row[:, 2, :], bank[1][0:1, 256:512], row[:, 1, :], ALU.subtract).then_inc(s_pre, 1)
            dve.wait_ge(s_pre, 15)
            dve.tensor_scalar(row[:, 3, :], row[:, 2, :], 1.0, 0.5, ALU.max, ALU.mult).then_inc(s_pre, 1)
            dve.wait_ge(s_pre, 16)
            dve.tensor_scalar(row[:, 3, :], row[:, 3, :], 0.25, 8388608.0, ALU.add, ALU.add).then_inc(s_pre, 1)
            dve.wait_ge(s_pre, 17)
            dve.tensor_scalar(row[:, 4, :], row[:, 3, :], -8388608.0, None, ALU.add).then_inc(s_pre, 1)
            dve.memset(row[:, 6, :], 1.0)
            dve.memset(row[:, 5, 0:1], 0.0)
            dve.wait_ge(s_wts, n_wts)
            for g in range(TPC):
                dve.tensor_copy(w1_rep[:, :, g, :].rearrange("p l (h o) -> p l h o", o=8),
                                w1_raw[:, :, g, :].unsqueeze(3).broadcast_to([TPC * NE10, 2, HID, 8]))
            dve.tensor_reduce(sel_base[:, :], ident[:, :].rearrange("p (h o) -> p o h", o=8), AX_X, ALU.add)\
                .then_inc(s_pre, 1)
            dve.wait_ge(s_pre, 19)
            dve.tensor_tensor_scan(row[:, 5, 1:256], row[:, 6, 0:255], row[:, 4, 0:255], 0.0,
                                   ALU.mult, ALU.add)
            dve.tensor_scalar(sel_layer1[:, :, :], sel_base[:, :].unsqueeze(1).broadcast_to([P, 4, 8]),
                              32 ** -0.5 * HID ** -0.5, None, ALU.mult)
            dve.tensor_scalar(sel_layer2[:, :], sel_base[:, :], 16 ** -0.5 * HID ** -0.5, None, ALU.mult)\
                .then_inc(s_pre, 1)
            dve.wait_ge(s_pre, 20)
            dve.scalar_tensor_tensor(out=table[:, 1, :], in0=row[:, 5, :], scalar=-2.0, in1=row[:, 1, :],
                                     op0=ALU.mult, op1=ALU.add)
            dve.tensor_copy(table[:, 0, :], row[:, 5, :]).then_inc(s_pre, 1)

            def prep(c, slot):
                dve.wait_ge(s_gath[slot], (c - slot) * 64 + 128)
                if not (isinstance(c, int) and c == 0):
                    dve.wait_ge(s_prep, c * 3)
                r4 = dirn[:, bass.ds(c * TPC, TPC), :]
                both = feat[:, slot, :, 0:2 * DF].rearrange("p g (a f) -> p g a f", a=2)
                for side in range(2):
                    ins = dve.tensor_tensor(
                        vdot_k[:, :, side, :, :],
                        both[:, :, side, 8:DF].rearrange("p g (u k) -> p g u k", k=3),
                        r4.unsqueeze(2).broadcast_to([P, TPC, 8, 3]), ALU.mult)
                ins.then_inc(s_prep, 1)
                dve.wait_ge(s_prep, c * 3 + 1)
                dve.tensor_reduce(feat[:, slot, :, 64:80], vdot_k[:, :, :, :, :].rearrange("p g a u k -> p g (a u) k"),
                                  AX_X, ALU.add).then_inc(s_prep, 1)
                sh = edge_in[:, bass.ds(c * TPC, TPC), NE10 + 1:NE10 + 4]
                for side in range(2):
                    ins = dve.tensor_tensor(
                        feat[:, slot, :, 80:128].rearrange("p g (k a u) -> p g k a u", k=3, a=2)[:, :, :, side, :],
                        both[:, :, side, 0:8].unsqueeze(2).broadcast_to([P, TPC, 3, 8]),
                        sh.unsqueeze(3).broadcast_to([P, TPC, 3, 8]), ALU.mult)
                ins.then_inc(s_prep, 1)

            def multiply(c, slot, b):
                n = c * NB + b
                dve.wait_ge(s_u, n + 1)
                if b in (0, 4):
                    dve.wait_ge(s_hidS, c * 2 + (1 if b == 0 else 2))
                if not (isinstance(c, int) and n < 3):
                    dve.wait_ge(s_red, n - 2)
                dve.tensor_tensor(prod[:, b % 3, :], bank[4 + (slot + b) % 2][:, :],
                                  hid[:, slot, 0 if b < 4 else 1, :], ALU.mult).then_inc(s_p, 1)

            def layer2_in(c, slot):
                dve.wait_ge(s_red, c * NB + 4)
                dve.wait_ge(s_scaleS, c + 1)
                dve.tensor_tensor(feat2[:, slot, :], bank[3][:, :], scale_t[:, slot, :], ALU.mult).then_inc(s_f2, 1)

            def output(c, slot):
                dve.wait_ge(s_tanh, c + 1)
                o2 = bank[6][:, 0:TPC * 40].rearrange("p (g c) -> p g c", g=TPC)
                nrm = nrm_row[:, bass.ds(c * TPC, TPC)].unsqueeze(2).broadcast_to([P, TPC, 8])
                dve.tensor_tensor(gate[:, slot, :, :], tanh_out[:, slot, :, 8:16], nrm, ALU.mult).then_inc(s_out, 1)
                dve.tensor_tensor(vals[:, bass.ds(c * TPC, TPC), 0:8], tanh_out[:, slot, :, 0:8], nrm, ALU.mult)\
                    .then_inc(s_out, 1)
                dve.wait_ge(s_out, c * 3 + 1)
                for k in range(3):
                    ins = dve.tensor_tensor(vals[:, bass.ds(c * TPC, TPC), 8 + k::3], o2[:, :, 16 + 8 * k:24 + 8 * k],
                                            gate[:, slot, :, :], ALU.mult)
                ins.then_inc(s_out, 1)

            def chunk(c, slot, before, nxt):
                multiply(c, slot, 0)
                multiply(c, slot, 1)
                if before:
                    output(c - 1, 1 - slot)
                if nxt:
                    prep(c + 1, 1 - slot)
                multiply(c, slot, 2)
                multiply(c, slot, 3)
                layer2_in(c, slot)
                for b in range(4, NB):
                    multiply(c, slot, b)

            prep(0, 0)
            chunk(0, 0, False, True)
            chunk(1, 1, True, True)
            with dve.Fori(1, NCH // 2) as i:
                chunk(i * 2, 0, True, True)
                chunk(i * 2 + 1, 1, True, True)
            chunk(NCH - 1, 0, True, False)
            output(NCH - 1, 0)
            dve.wait_ge(s_pre, 21)

            def onehots(s, slot, nwin):
                for w in range(nwin):
                    n0 = dve.value_load(table[0:1, 0, bass.ds(s * WPS + w, 1)], min_val=0, max_val=NT * NW)
                    n1 = dve.value_load(table[0:1, 0, bass.ds(s * WPS + w + 1, 1)], min_val=1, max_val=NT * NW)
                    off = dve.value_load(table[0:1, 1, bass.ds(s * WPS + w, 1)], min_val=-2 * NT * NW, max_val=NT)
                    with dve.Fori(n0, n1) as n:
                        t = nc.s_assert_within(dve.snap(n * 2 + off), 0, NT,
                                              skip_runtime_bounds_check_because="the table's tiles lie in [0, NT)")
                        for h in range(2):
                            dve.wait_ge(s_ohused[h], n + 1)
                            dve.tensor_scalar(onehot[:, h, :], node_of_col[:, :],
                                              window_base[:, bass.ds(s * WPS + w, 1)],
                                              dst_row[:, bass.ds(t + h, 1)],
                                              ALU.add, ALU.is_equal).then_inc(s_oh[h], 1)

            def norm_a(s, slot, nwin, first, nloads):
                done = dve.value_load(table[0:1, 0, bass.ds(s * WPS + nwin, 1)], min_val=1, max_val=NT * NW)
                dve.wait_ge(s_ohused[0], done + 1)
                dve.wait_ge(s_ohused[1], done + 1)
                dve.wait_ge(s_x[slot], (s - slot) * 8 + 16 * nloads)
                if not first:
                    dve.wait_ge(s_cent, s - 1)
                dve.tensor_tensor(ysum[:, slot, :, :].rearrange("p a b -> p (a b)"), bank[slot][:, :],
                                  xin[:, slot, :, :].rearrange("p a b -> p (a b)"), ALU.add).then_inc(s_y, 1)
                dve.wait_ge(s_y, s + 1)
                dve.tensor_reduce(mean[:, slot, :], ysum[:, slot, :, :], AX_X, ALU.add).then_inc(s_sum, 1)
                dve.wait_ge(s_sum, s + 1)
                dve.tensor_scalar(nmean[:, slot, :], mean[:, slot, :], -1.0 / DF, None, ALU.mult).then_inc(s_mean, 1)

            def norm_b(s, slot, first):
                dve.wait_ge(s_csq, s + 1)
                if not first:
                    dve.wait_ge(s_sd, s - 1)
                dve.tensor_reduce(var[:, slot, :], csq[:, slot, :, :], AX_X, ALU.add).then_inc(s_var, 1)

            def norm_c(s, slot, first):
                dve.wait_ge(s_sd, s + 1)
                if not first:
                    dve.wait_ge(s_yout, s - 1)
                dve.reciprocal(rstd[:, slot, :], stdev[:, slot, :]).then_inc(s_rstd, 1)

            onehots(0, 0, WPS)
            norm_a(0, 0, WPS, True, 1)
            onehots(1, 1, WPS)
            norm_a(1, 1, WPS, True, 1)
            norm_b(0, 0, True)
            onehots(2, 0, WPS)
            norm_a(2, 0, WPS, False, 1)
            norm_c(0, 0, True)
            norm_b(1, 1, True)
            onehots(3, 1, WPS)
            norm_a(3, 1, WPS, False, 1)
            norm_c(1, 1, True)
            norm_b(2, 0, False)
            with dve.Fori(2, (NS - 1) // 2) as i:
                for slot in range(2):
                    onehots(i * 2 + slot, slot, WPS)
                    norm_a(i * 2 + slot, slot, WPS, False, 1)
                    norm_c(i * 2 + slot - 2, slot, False)
                    norm_b(i * 2 + slot - 1, 1 - slot, False)
            left = NW - (NS - 1) * WPS
            onehots(NS - 1, 0, left)
            norm_a(NS - 1, 0, left, False, 2)
            norm_c(NS - 3, 0, False)
            norm_b(NS - 2, 1, False)
            norm_c(NS - 2, 1, False)
            norm_b(NS - 1, 0, False)
            norm_c(NS - 1, 0, False)


_INS = ['x', 'src', 'dst', 'edge_attr_10', 'edge_attr_3', 'edge_weight',
        'L0_gnn_fc1_w1', 'L0_gnn_fc1_w2', 'L0_gnn_fc2_w1', 'L0_gnn_fc2_w2']
_OUTS = [((100000, 32), 'float32')]


def kernel(**inputs):
    import numpy as _np
    import concourse.bacc as _bacc
    from concourse import mybir as _mybir
    from concourse.bass_utils import run_bass_kernel_spmd as _run

    nc = _bacc.Bacc("TRN2", target_bir_lowering=False, num_devices=1)
    arrays, args = {}, []
    for name in _INS:
        a = _np.ascontiguousarray(inputs[name])
        arrays[f"in_{name}_dram"] = a
        args.append(nc.dram_tensor(f"in_{name}_dram", a.shape, _mybir.dt.from_np(a.dtype), kind="ExternalInput").ap())
    for i, (shape, dtype) in enumerate(_OUTS):
        dt = _mybir.dt.from_np(_np.dtype(dtype))
        args.append(nc.dram_tensor(f"out_{i}_dram", shape, dt, kind="ExternalOutput").ap())
    gnn_layernorm(nc, *args)
    r = _run(nc, [arrays], core_ids=[0])
    got = tuple(r.results[0][f"out_{i}_dram"] for i in range(len(_OUTS)))
    return got[0]
```
